# Optimizing a Trainium2 kernel written in Bass

```python
import numpy as np
import jax
import jax.numpy as jnp

def _softmax(x, axis=-1):
    return jax.nn.softmax(x, axis=axis)

def _gelu(x):
    return jax.nn.gelu(x, approximate=True)

def _silu(x):
    return jax.nn.silu(x)

def _sigmoid(x):
    return jax.nn.sigmoid(x)

def _layernorm(x, axis=-1, eps=1e-05):
    m = jnp.mean(x, axis=axis, keepdims=True)
    v = jnp.var(x, axis=axis, keepdims=True)
    return (x - m) / jnp.sqrt(v + eps)

def _scatter_add(tgt, idx, src, axis=0):
    return tgt.at[idx].add(src)

def _segment_sum(src, seg, n):
    return jax.ops.segment_sum(src, seg, n)
kernel_name = 'mk_dlrm_tower_d1_rec_r8_1bae0b'

def setup_inputs(seed: int=0):
    np.random.seed(seed)
    _w = jnp.asarray

    def _rec_inputs():
        import jax
        import jax.numpy as jnp
        _tk = jax.random.key(seed)
        ids = jnp.stack([jax.random.randint(jax.random.fold_in(_tk, 200 + f), (512,), 0, v, jnp.int32) for f, v in enumerate([1250, 125000, 12500, 1000, 12500, 12500, 1000, 1250, 1000, 1250, 12500, 1250, 12500, 1000, 12500, 12500, 1000, 12500, 12500, 1000, 1000, 1000, 1000, 1000, 1000, 1000])], axis=1)
        tbl_0 = 0.05 * jax.random.normal(jax.random.fold_in(_tk, 500 + 0), (1250, 128), jnp.float32)
        tbl_1 = 0.05 * jax.random.normal(jax.random.fold_in(_tk, 500 + 1), (125000, 128), jnp.float32)
        tbl_2 = 0.05 * jax.random.normal(jax.random.fold_in(_tk, 500 + 2), (12500, 128), jnp.float32)
        tbl_3 = 0.05 * jax.random.normal(jax.random.fold_in(_tk, 500 + 3), (1000, 128), jnp.float32)
        tbl_4 = 0.05 * jax.random.normal(jax.random.fold_in(_tk, 500 + 4), (12500, 128), jnp.float32)
        tbl_5 = 0.05 * jax.random.normal(jax.random.fold_in(_tk, 500 + 5), (12500, 128), jnp.float32)
        tbl_6 = 0.05 * jax.random.normal(jax.random.fold_in(_tk, 500 + 6), (1000, 128), jnp.float32)
        tbl_7 = 0.05 * jax.random.normal(jax.random.fold_in(_tk, 500 + 7), (1250, 128), jnp.float32)
        tbl_8 = 0.05 * jax.random.normal(jax.random.fold_in(_tk, 500 + 8), (1000, 128), jnp.float32)
        tbl_9 = 0.05 * jax.random.normal(jax.random.fold_in(_tk, 500 + 9), (1250, 128), jnp.float32)
        tbl_10 = 0.05 * jax.random.normal(jax.random.fold_in(_tk, 500 + 10), (12500, 128), jnp.float32)
        tbl_11 = 0.05 * jax.random.normal(jax.random.fold_in(_tk, 500 + 11), (1250, 128), jnp.float32)
        tbl_12 = 0.05 * jax.random.normal(jax.random.fold_in(_tk, 500 + 12), (12500, 128), jnp.float32)
        tbl_13 = 0.05 * jax.random.normal(jax.random.fold_in(_tk, 500 + 13), (1000, 128), jnp.float32)
        tbl_14 = 0.05 * jax.random.normal(jax.random.fold_in(_tk, 500 + 14), (12500, 128), jnp.float32)
        tbl_15 = 0.05 * jax.random.normal(jax.random.fold_in(_tk, 500 + 15), (12500, 128), jnp.float32)
        tbl_16 = 0.05 * jax.random.normal(jax.random.fold_in(_tk, 500 + 16), (1000, 128), jnp.float32)
        tbl_17 = 0.05 * jax.random.normal(jax.random.fold_in(_tk, 500 + 17), (12500, 128), jnp.float32)
        tbl_18 = 0.05 * jax.random.normal(jax.random.fold_in(_tk, 500 + 18), (12500, 128), jnp.float32)
        tbl_19 = 0.05 * jax.random.normal(jax.random.fold_in(_tk, 500 + 19), (1000, 128), jnp.float32)
        tbl_20 = 0.05 * jax.random.normal(jax.random.fold_in(_tk, 500 + 20), (1000, 128), jnp.float32)
        tbl_21 = 0.05 * jax.random.normal(jax.random.fold_in(_tk, 500 + 21), (1000, 128), jnp.float32)
        tbl_22 = 0.05 * jax.random.normal(jax.random.fold_in(_tk, 500 + 22), (1000, 128), jnp.float32)
        tbl_23 = 0.05 * jax.random.normal(jax.random.fold_in(_tk, 500 + 23), (1000, 128), jnp.float32)
        tbl_24 = 0.05 * jax.random.normal(jax.random.fold_in(_tk, 500 + 24), (1000, 128), jnp.float32)
        tbl_25 = 0.05 * jax.random.normal(jax.random.fold_in(_tk, 500 + 25), (1000, 128), jnp.float32)
        _rk = jax.random.fold_in(_tk, 7)
        r_dense_features = -0.000520686 + 1.00062 * jax.random.normal(jax.random.fold_in(_rk, 101), (512, 128), jnp.float32)
        W_top1 = 0.0405887 * jax.random.normal(jax.random.fold_in(_tk, 801), (607, 512), jnp.float32)
        W_top2 = 0.0441942 * jax.random.normal(jax.random.fold_in(_tk, 802), (512, 256), jnp.float32)
        W_top3 = 0.0625 * jax.random.normal(jax.random.fold_in(_tk, 803), (256, 1), jnp.float32)
        b_top1 = jnp.zeros((512,), jnp.float32)
        b_top2 = jnp.zeros((256,), jnp.float32)
        return (r_dense_features, ids, tbl_0, tbl_1, tbl_2, tbl_3, tbl_4, tbl_5, tbl_6, tbl_7, tbl_8, tbl_9, tbl_10, tbl_11, tbl_12, tbl_13, tbl_14, tbl_15, tbl_16, tbl_17, tbl_18, tbl_19, tbl_20, tbl_21, tbl_22, tbl_23, tbl_24, tbl_25, W_top1, b_top1, W_top2, b_top2, W_top3)
    r_dense_features, ids, tbl_0, tbl_1, tbl_2, tbl_3, tbl_4, tbl_5, tbl_6, tbl_7, tbl_8, tbl_9, tbl_10, tbl_11, tbl_12, tbl_13, tbl_14, tbl_15, tbl_16, tbl_17, tbl_18, tbl_19, tbl_20, tbl_21, tbl_22, tbl_23, tbl_24, tbl_25, W_top1, b_top1, W_top2, b_top2, W_top3 = _rec_inputs()

    def _L0_rec_setup():
        import jax, jax.numpy as jnp
        import numpy as np
        F = 26
        B, D = (2048, 128)
        _IU0, _IU1 = np.triu_indices(F + 1, k=1)
        _IU0 = jnp.asarray(_IU0)
        _IU1 = jnp.asarray(_IU1)
        key = jax.random.key(seed)
        k1, k2 = jax.random.split(key)
        dense_features = jax.random.normal(k1, (B, D), dtype=jnp.float32)
        sparse_features = jax.random.normal(k2, (B, F, D), dtype=jnp.float32)
        return {'dense_features': dense_features, 'sparse_features': sparse_features}
    _L0_rec_all = _L0_rec_setup()
    _L0_rec_in = {k: v for k, v in _L0_rec_all.items() if k in ()}
    del _L0_rec_all
    return {'r_dense_features': r_dense_features, 'ids': ids, 'tbl_0': tbl_0, 'tbl_1': tbl_1, 'tbl_2': tbl_2, 'tbl_3': tbl_3, 'tbl_4': tbl_4, 'tbl_5': tbl_5, 'tbl_6': tbl_6, 'tbl_7': tbl_7, 'tbl_8': tbl_8, 'tbl_9': tbl_9, 'tbl_10': tbl_10, 'tbl_11': tbl_11, 'tbl_12': tbl_12, 'tbl_13': tbl_13, 'tbl_14': tbl_14, 'tbl_15': tbl_15, 'tbl_16': tbl_16, 'tbl_17': tbl_17, 'tbl_18': tbl_18, 'tbl_19': tbl_19, 'tbl_20': tbl_20, 'tbl_21': tbl_21, 'tbl_22': tbl_22, 'tbl_23': tbl_23, 'tbl_24': tbl_24, 'tbl_25': tbl_25, 'W_top1': W_top1, 'b_top1': b_top1, 'W_top2': W_top2, 'b_top2': b_top2, 'W_top3': W_top3}

def reference(r_dense_features, ids, tbl_0, tbl_1, tbl_2, tbl_3, tbl_4, tbl_5, tbl_6, tbl_7, tbl_8, tbl_9, tbl_10, tbl_11, tbl_12, tbl_13, tbl_14, tbl_15, tbl_16, tbl_17, tbl_18, tbl_19, tbl_20, tbl_21, tbl_22, tbl_23, tbl_24, tbl_25, W_top1, b_top1, W_top2, b_top2, W_top3):
    import jax
    import jax.numpy as jnp

    def _L0_rec_ref(dense_features, sparse_features):
        import jax, jax.numpy as jnp
        import numpy as np
        F = 26
        B, D = (2048, 128)
        _IU0, _IU1 = np.triu_indices(F + 1, k=1)
        _IU0 = jnp.asarray(_IU0)
        _IU1 = jnp.asarray(_IU1)
        combined = jnp.concatenate([dense_features[:, None, :], sparse_features], axis=1)
        interactions = jnp.einsum('bfd,bgd->bfg', combined, combined)
        interactions_flat = interactions[:, _IU0, _IU1]
        return jnp.concatenate([dense_features, interactions_flat], axis=1)
    e = jnp.stack([tbl_0[ids[:, 0]], tbl_1[ids[:, 1]], tbl_2[ids[:, 2]], tbl_3[ids[:, 3]], tbl_4[ids[:, 4]], tbl_5[ids[:, 5]], tbl_6[ids[:, 6]], tbl_7[ids[:, 7]], tbl_8[ids[:, 8]], tbl_9[ids[:, 9]], tbl_10[ids[:, 10]], tbl_11[ids[:, 11]], tbl_12[ids[:, 12]], tbl_13[ids[:, 13]], tbl_14[ids[:, 14]], tbl_15[ids[:, 15]], tbl_16[ids[:, 16]], tbl_17[ids[:, 17]], tbl_18[ids[:, 18]], tbl_19[ids[:, 19]], tbl_20[ids[:, 20]], tbl_21[ids[:, 21]], tbl_22[ids[:, 22]], tbl_23[ids[:, 23]], tbl_24[ids[:, 24]], tbl_25[ids[:, 25]]], axis=1)
    z = _L0_rec_ref(r_dense_features, e)
    z = z.reshape(z.shape[0], -1)
    h = jnp.concatenate([z, r_dense_features], axis=1)
    h = jnp.maximum(h @ W_top1 + b_top1, 0.0)
    h = jnp.maximum(h @ W_top2 + b_top2, 0.0)
    y = h @ W_top3
    return y

_drawn_inputs = setup_inputs


def setup_inputs(seed=0):
    import zlib

    import numpy as np

    out = dict(_drawn_inputs(seed))
    spreads = {'b_top1': (0.0, 0.1), 'b_top2': (0.0, 0.1)}
    factors = {}
    for name, (base, spread) in spreads.items():
        noise = np.random.default_rng([zlib.crc32(name.encode()), seed]).standard_normal(out[name].shape)
        drawn = base * np.exp(spread * noise) if base else spread * noise
        out[name] = jnp.asarray(drawn.astype(out[name].dtype))
    for name, factor in factors.items():
        out[name] = (out[name] * factor).astype(out[name].dtype)
    return out
```

```python
import numpy as np
import concourse.bass as bass
from concourse import mybir
from contextlib import ExitStack

F32 = mybir.dt.float32
F32R = mybir.dt.float32r
I32 = mybir.dt.int32
ALU = mybir.AluOpType
ACT = mybir.ActivationFunctionType

B, D, NT = 512, 128, 26
ROWS = [1250, 125000, 12500, 1000, 12500, 12500, 1000, 1250, 1000, 1250, 12500, 1250, 12500, 1000,
        12500, 12500, 1000, 12500, 12500, 1000, 1000, 1000, 1000, 1000, 1000, 1000]
N_ONEHOT = 9
SMALL = [f for f in range(NT) if ROWS[f] == 1000]
ONEHOT = SMALL[len(SMALL) - N_ONEHOT:]
GATHERED = [f for f in range(NT) if f not in ONEHOT]
NG = len(GATHERED)
F = NT + 1
SLOTS = [0] + [f + 1 for f in GATHERED + ONEHOT]
TILES = B // 128
CHUNK = 4
CHUNKS = [(c, min(c + CHUNK, NG + 1)) for c in range(0, NG + 1, CHUNK)]
NC_T = len(CHUNKS)
R = 8
GRP = 32
FP = F - 1
PW = 4 * FP
BANKS = GRP // 4
BLOCKS = [(g, min(8, FP - g), FP - g) for g in range(0, FP, 8)]
ZOFF = [sum(n * w for _, n, w in BLOCKS[:i]) for i in range(len(BLOCKS) + 1)]
ZC = -(-ZOFF[-1] // 128)
H1, H2 = 512, 256
N1, N2 = H1 // 128, H2 // 128


def schedule():
    steps, q = [], 0
    for i in range(N_ONEHOT):
        steps += [("onehot", i), ("chunk", q)]
        q += 1
    for t in range(TILES):
        while q < NC_T * (t + 1):
            steps.append(("chunk", q))
            q += 1
        for b in range(BANKS):
            steps.append(("gram", t, b))
            if t > 0 and b % 2 == 0:
                steps.append((["fold", "top1", "top2", "top3"][b // 2], t - 1))
            if t < TILES - 1 and b % 2 == 1 and q < NC_T * (t + 2):
                steps.append(("chunk", q))
                q += 1
        for k in range(len(BLOCKS)):
            steps.append(("turn", t, k))
    return steps + [(s, TILES - 1) for s in ("fold", "top1", "top2", "top3")]


STEPS = schedule()
XG_RING = 7
OH_RING = 10
TAB_RING = 3


def build(nc, tables, onehot_tables, gather_ids, onehot_ids, dense, w1z, w1d, w2, w3, b1, b2, out):
    with ExitStack() as ctx:
        def sb(name, shape, dt=F32):
            return ctx.enter_context(nc.sbuf_tensor(name, shape, dt))

        def sem(name):
            return ctx.enter_context(nc.semaphore(name))

        xh = sb("xh", [128, TILES, GRP, F, 4], F32R)
        xl = sb("xl", [128, TILES, GRP, F, 4], F32R)
        stage = sb("stage", [128, TAB_RING * (R * D + B)])
        tab = [stage[:, i * R * D:(i + 1) * R * D] for i in range(TAB_RING)]
        ids0 = TAB_RING * R * D
        tab_ids = [stage[:, ids0 + i * B:ids0 + (i + 1) * B].bitcast(I32) for i in range(TAB_RING)]
        gcols = GRP * FP * 4
        gram_sb = stage[0:PW, 0:gcols].rearrange("p (c j) -> p c j", j=GRP)
        z = stage[:, gcols:gcols + 128 * ZC]
        zT = stage[:, gcols + 128 * ZC:gcols + 256 * ZC].rearrange("p (c b) -> p c b", b=128)
        th = sb("th", [128, 2, R, D], F32R)
        tl = sb("tl", [128, 2, R, D], F32R)
        oh = sb("oh", [128, OH_RING, B], F32R)
        xg = sb("xg", [128, XG_RING, CHUNK, D])
        dn = sb("dn", [128, TILES, D])
        dnT = sb("dnT", [128, TILES, 128])
        gids = sb("gids", [128, TILES * NG], I32)
        w1z_sb = sb("w1z_sb", [128, ZC, H1])
        w1d_sb = sb("w1d_sb", [128, 2, H1])
        w2_sb = sb("w2_sb", [128, N1, H2])
        small = sb("small", [128, N2 + N1 + N2])
        w3_sb, b1_sb, b2_sb = small[:, 0:N2], small[:, N2:N2 + N1], small[:, N2 + N1:]
        h1 = sb("h1", [128, N1, 128])
        h2 = sb("h2", [128, N2, 128])
        ident = sb("ident", [128, 128])
        rowno = sb("rowno", [128, R])
        y = sb("y", [1, B])

        wide = [ctx.enter_context(nc.psum_tensor(f"wide{i}", [128, 1024], F32)) for i in range(2)]
        flip = ctx.enter_context(nc.psum_tensor("flip", [128, 512], F32))
        prod = [ctx.enter_context(nc.psum_tensor(f"prod{i}", [128, 512], F32)) for i in range(2)]
        mlp = ctx.enter_context(nc.psum_tensor("mlp", [128, 512], F32))

        gids_in, dense_in, w1_in, w2_in, small_in = map(sem, ("gids_in", "dense_in", "w1_in", "w2_in", "small_in"))
        tab_in = [sem(f"tab_in{i}") for i in range(TAB_RING)]
        xg_in = [sem(f"xg_in{i}") for i in range(XG_RING)]
        ident_zero, ident_ready, rowno_ready = sem("ident_zero"), sem("ident_ready"), sem("rowno_ready")
        th_ready, tl_ready, oh_ready = sem("th_ready"), sem("tl_ready"), sem("oh_ready")
        oh_used, oh_out = sem("oh_used"), sem("oh_out")
        flipped, hi_ready, lo_ready = sem("flipped"), sem("hi_ready"), sem("lo_ready")
        prod_done, prod_out_act, prod_out_dve = sem("prod_done"), sem("prod_out_act"), sem("prod_out_dve")
        turned, z_act, z_dve = sem("turned"), sem("z_act"), sem("z_dve")
        z_pad, wd_ready = sem("z_pad"), sem("wd_ready")
        folded, zT_ready = sem("folded"), sem("zT_ready")
        top1_done, h1_ready, top2_done, h2_ready = map(sem, ("top1_done", "h1_ready", "top2_done", "h2_ready"))
        top3_done, y_ready, y_out = sem("top3_done"), sem("y_ready"), sem("y_out")

        def gathers_before(q):
            return sum(CHUNKS[k % NC_T][1] - max(CHUNKS[k % NC_T][0], 1) for k in range(q % XG_RING, q + 1, XG_RING))

        block = ctx.enter_context(nc.Block())

        @block.sync
        def _(sp):
            sp.dma_start(gids[:, :], gather_ids).then_inc(gids_in, 16)

            def load_table(i):
                if i >= TAB_RING:
                    sp.wait_ge(tl_ready, i - TAB_RING + 1)
                    sp.wait_ge(oh_ready, R * (i - TAB_RING + 1))
                sp.dma_start(tab_ids[i % TAB_RING],
                             onehot_ids[i:i + 1, :].to_broadcast((128, B))).then_inc(tab_in[i % TAB_RING], 16)
                sp.dma_start(tab[i % TAB_RING], onehot_tables[i]).then_inc(tab_in[i % TAB_RING], 16)

            load_table(0)
            load_table(1)
            sp.dma_start(dn[:, :, :], dense).then_inc(dense_in, 16)
            load_table(2)
            sp.dma_start(w1d_sb[:, :, :], w1d).then_inc(w1_in, 16)
            sp.dma_start(w1z_sb[:, :, :], w1z).then_inc(w1_in, 16)
            sp.dma_start(w2_sb[:, :, :], w2).then_inc(w2_in, 16)
            sp.dma_start(w3_sb, w3).then_inc(small_in, 16)
            sp.dma_start(b1_sb, b1).then_inc(small_in, 16)
            sp.dma_start(b2_sb, b2).then_inc(small_in, 16)
            for i in range(TAB_RING, N_ONEHOT):
                load_table(i)
            sp.wait_ge(y_ready, TILES)
            sp.dma_start(out, y[:, :]).then_inc(y_out, 16)
            sp.wait_ge(y_out, 16)

        @block.gpsimd
        def _(pool):
            nc.gpsimd.iota(rowno[:, :], [[1, R]], base=0, channel_multiplier=R,
                           allow_small_or_imprecise_dtypes=True).then_inc(rowno_ready, 1)
            nc.gpsimd.memset(ident[:, :], 0.0).then_inc(ident_zero, 1)
            pool.wait_ge(ident_zero, 1)
            nc.gpsimd.affine_select(out=ident[:, :], in_=ident[:, :], compare_op=ALU.not_equal, fill=1.0, base=0,
                                    pattern=[[-1, 128]], channel_multiplier=1).then_inc(ident_ready, 1)
            pool.wait_ge(gids_in, 16)
            for q in range(TILES * NC_T):
                t, (lo, hi) = q // NC_T, CHUNKS[q % NC_T]
                if q >= XG_RING:
                    pool.wait_ge(flipped, q - XG_RING + 1)
                for s in range(max(lo, 1), hi):
                    n = t * NG + s - 1
                    pool.indirect_dma_start(xg[:, q % XG_RING, s - lo, :], None, tables[s - 1],
                                            bass.IndirectOffsetOnAxis(ap=gids[:, n:n + 1], axis=0)
                                            ).then_inc(xg_in[q % XG_RING], 16)

        @block.scalar
        def _(act):
            def table_hi(i):
                act.wait_ge(tab_in[i % TAB_RING], 32 * (i // TAB_RING + 1))
                if i >= 2:
                    act.wait_ge(oh_used, R * (i - 1))
                nc.scalar.copy(th[:, i % 2, :, :], tab[i % TAB_RING].rearrange("p (r d) -> p r d", d=D)
                               ).then_inc(th_ready, 1)

            table_hi(0)
            for step in STEPS:
                kind, t = step[0], step[1]
                if kind == "onehot":
                    if t + 1 < N_ONEHOT:
                        table_hi(t + 1)
                    act.wait_ge(oh_used, R * (t + 1))
                    slot = NG + 1 + t
                    src = wide[t % 2]
                    nc.scalar.copy(xh[:, :, :, slot, :].rearrange("p t j s -> p (t j) s"),
                                   src[:, 0:B].rearrange("p (j s) -> p j s", s=4))
                    nc.scalar.copy(xl[:, :, :, slot, :].rearrange("p t j s -> p (t j) s"),
                                   src[:, B:2 * B].rearrange("p (j s) -> p j s", s=4)).then_inc(oh_out, 1)
                elif kind == "chunk":
                    q, tile, (lo, hi) = t, t // NC_T, CHUNKS[t % NC_T]
                    act.wait_ge(flipped, q + 1)
                    if lo == 0:
                        nc.scalar.copy(dnT[:, tile, :], flip[:, 0:128])
                    nc.scalar.copy(xh[:, tile, :, lo:hi, :].rearrange("p j f s -> p f j s"),
                                   flip[:, 0:128 * (hi - lo)].rearrange("p (f j s) -> p f j s", j=GRP, s=4)).then_inc(hi_ready, 1)
                elif kind == "gram" and step[2] % 2:
                    b = step[2]
                    act.wait_ge(prod_done, BANKS * t + b + 1)
                    if t: act.wait_ge(turned, len(BLOCKS) * t)
                    nc.scalar.copy(gram_sb[:, :, 4 * b:4 * b + 4],
                                   prod[b % 2][0:PW, 0:4 * PW].rearrange("p (j c) -> p c j", j=4)
                                   ).then_inc(prod_out_act, 1)
                elif kind == "turn":
                    k = step[2]
                    g0, n, w = BLOCKS[k]
                    act.wait_ge(turned, len(BLOCKS) * t + k + 1)
                    if t:
                        act.wait_ge(folded, t)
                    else:
                        act.wait_ge(z_pad, 1)
                    for s in (0, 1):
                        last = nc.scalar.copy(
                            z[32 * s:32 * s + 32, ZOFF[k]:ZOFF[k + 1]].rearrange("p (g f) -> p g f", f=w),
                            wide[k % 2][32 * s:32 * s + 32, 0:128 * n].rearrange("p (g c) -> p g c", c=128)
                            [:, :, 4 * g0 + s:PW:4])
                    last.then_inc(z_act, 1)
                elif kind == "fold":
                    act.wait_ge(folded, t + 1)
                    nc.scalar.copy(zT, mlp[:, 0:128 * ZC].rearrange("p (c b) -> p c b", b=128)).then_inc(zT_ready, 1)
                elif kind == "top1":
                    act.wait_ge(top1_done, t + 1)
                    act.wait_ge(small_in, 48)
                    for n in range(N1):
                        last = nc.scalar.activation(h1[:, n, :], mlp[:, 128 * n:128 * n + 128], ACT.Relu,
                                                    bias=b1_sb[:, n:n + 1])
                    last.then_inc(h1_ready, 1)
                elif kind == "top2":
                    act.wait_ge(top2_done, t + 1)
                    for m in range(N2):
                        last = nc.scalar.activation(h2[:, m, :], mlp[:, 128 * m:128 * m + 128], ACT.Relu,
                                                    bias=b2_sb[:, m:m + 1])
                    last.then_inc(h2_ready, 1)
                elif kind == "top3":
                    act.wait_ge(top3_done, t + 1)
                    nc.scalar.copy(y[:, 128 * t:128 * t + 128], mlp[0:1, 0:128]).then_inc(y_ready, 1)

        @block.vector
        def _(dve):
            def build_onehot(i):
                place = i % TAB_RING
                dve.wait_ge(th_ready, i + 1)
                if i >= 2:
                    dve.wait_ge(oh_used, R * (i - 1))
                nc.vector.tensor_tensor(tl[:, i % 2, :, :], tab[place].rearrange("p (r d) -> p r d", d=D),
                                        th[:, i % 2, :, :].bitcast(F32), ALU.subtract).then_inc(tl_ready, 1)
                for j in range(R):
                    n = R * i + j
                    if n >= OH_RING:
                        dve.wait_ge(oh_used, n - OH_RING + 1)
                    nc.vector.tensor_scalar(oh[:, n % OH_RING, :], tab_ids[place], rowno[:, j:j + 1], None,
                                            ALU.is_equal).then_inc(oh_ready, 1)

            dve.wait_ge(rowno_ready, 1)
            build_onehot(0)
            for step in STEPS:
                kind, t = step[0], step[1]
                if kind == "onehot":
                    if t + 1 < N_ONEHOT:
                        build_onehot(t + 1)
                elif kind == "chunk":
                    q, tile, (lo, hi) = t, t // NC_T, CHUNKS[t % NC_T]
                    dve.wait_ge(hi_ready, q + 1)
                    nc.vector.tensor_tensor(xl[:, tile, :, lo:hi, :].rearrange("p j f s -> p f j s"),
                                            flip[:, 0:128 * (hi - lo)].rearrange("p (f j s) -> p f j s", j=GRP, s=4),
                                            xh[:, tile, :, lo:hi, :].rearrange("p j f s -> p f j s").bitcast(F32),
                                            ALU.subtract).then_inc(lo_ready, 1)
                    if q == N_ONEHOT:
                        dve.wait_ge(w1_in, 32)
                        nc.vector.tensor_tensor(w1d_sb[:, 0, :], w1d_sb[:, 0, :], w1d_sb[:, 1, :], ALU.add
                                                ).then_inc(wd_ready, 1)
                        dve.wait_ge(oh_used, R * N_ONEHOT)
                        nc.vector.memset(z[:, ZOFF[-1]:128 * ZC], 0.0).then_inc(z_pad, 1)
                elif kind == "gram" and step[2] % 2 == 0:
                    b = step[2]
                    dve.wait_ge(prod_done, BANKS * t + b + 1)
                    if t: dve.wait_ge(turned, len(BLOCKS) * t)
                    nc.vector.tensor_copy(gram_sb[:, :, 4 * b:4 * b + 4],
                                          prod[b % 2][0:PW, 0:4 * PW].rearrange("p (j c) -> p c j", j=4)
                                          ).then_inc(prod_out_dve, 1)
                elif kind == "turn":
                    k = step[2]
                    g0, n, w = BLOCKS[k]
                    dve.wait_ge(turned, len(BLOCKS) * t + k + 1)
                    if t:
                        dve.wait_ge(folded, t)
                    for s in (2, 3):
                        last = nc.vector.tensor_copy(
                            z[32 * s:32 * s + 32, ZOFF[k]:ZOFF[k + 1]].rearrange("p (g f) -> p g f", f=w),
                            wide[k % 2][32 * s:32 * s + 32, 0:128 * n].rearrange("p (g c) -> p g c", c=128)
                            [:, :, 4 * g0 + s:PW:4])
                    last.then_inc(z_dve, 1)

        @block.tensor
        def _(pe):
            pe.wait_ge(ident_ready, 1)
            for step in STEPS:
                kind, t = step[0], step[1]
                if kind == "onehot":
                    pe.wait_ge(tl_ready, t + 1)
                    if t >= 2:
                        pe.wait_ge(oh_out, t - 1)
                    acc = wide[t % 2]
                    for j in range(R):
                        n = R * t + j
                        pe.wait_ge(oh_ready, n + 1)
                        nc.tensor.matmul(acc[:, 0:B], th[:, t % 2, j, :], oh[:, n % OH_RING, :],
                                         start=(j == 0), stop=(j == R - 1))
                        nc.tensor.matmul(acc[:, B:2 * B], tl[:, t % 2, j, :], oh[:, n % OH_RING, :],
                                         start=(j == 0), stop=(j == R - 1)).then_inc(oh_used, 1)
                elif kind == "chunk":
                    q, tile, (lo, hi) = t, t // NC_T, CHUNKS[t % NC_T]
                    pe.wait_ge(xg_in[q % XG_RING], 16 * gathers_before(q))
                    if q == 0:
                        pe.wait_ge(dense_in, 16)
                    if q >= 1:
                        pe.wait_ge(lo_ready, q)
                    for s in range(lo, hi):
                        src = dn[:, tile, :] if s == 0 else xg[:, q % XG_RING, s - lo, :]
                        last = nc.tensor.transpose(flip[:, 128 * (s - lo):128 * (s - lo) + 128], src, ident[:, :])
                    last.then_inc(flipped, 1)
                elif kind == "gram":
                    b = step[2]
                    if b == 0:
                        pe.wait_ge(lo_ready, NC_T * (t + 1))
                        pe.wait_ge(oh_out, N_ONEHOT)
                    if BANKS * t + b >= 2:
                        pe.wait_ge(prod_out_act if b % 2 else prod_out_dve, (BANKS * t + b) // 2)
                    for j in range(4 * b, 4 * b + 4):
                        dst = prod[b % 2][0:PW, PW * (j % 4):PW * (j % 4) + PW]
                        sth, stl = (x[:, t, j, 1:F, :].rearrange("p f s -> p (f s)") for x in (xh, xl))
                        mvh, mvl = (x[:, t, j, 0:FP, :].rearrange("p f s -> p (f s)") for x in (xh, xl))
                        nc.tensor.matmul(dst, sth, mvh, start=True, stop=False)
                        nc.tensor.matmul(dst, sth, mvl, start=False, stop=False)
                        last = nc.tensor.matmul(dst, stl, mvh, start=False, stop=True)
                    last.then_inc(prod_done, 1)
                elif kind == "turn":
                    k = step[2]
                    n0 = len(BLOCKS) * t + k
                    if k == 0:
                        pe.wait_ge(prod_out_act, BANKS // 2 * (t + 1))
                        pe.wait_ge(prod_out_dve, BANKS // 2 * (t + 1))
                    if n0 >= 2:
                        pe.wait_ge(z_act, n0 - 1)
                        pe.wait_ge(z_dve, n0 - 1)
                    g0, n, w = BLOCKS[k]
                    for g in range(n):
                        last = nc.tensor.transpose(wide[k % 2][:, 128 * g:128 * g + PW],
                                                   gram_sb[:, 4 * (g0 + g):4 * (g0 + g) + 4, :].rearrange("p s j -> p (s j)"),
                                                   ident[0:PW, 0:PW])
                    last.then_inc(turned, 1)
                elif kind == "fold":
                    pe.wait_ge(z_act, len(BLOCKS) * (t + 1))
                    pe.wait_ge(z_dve, len(BLOCKS) * (t + 1))
                    if t:
                        pe.wait_ge(y_ready, t)
                    for c in range(ZC):
                        last = nc.tensor.transpose(mlp[:, 128 * c:128 * c + 128], z[:, 128 * c:128 * c + 128],
                                                   ident[:, :])
                    last.then_inc(folded, 1)
                elif kind == "top1":
                    pe.wait_ge(zT_ready, t + 1)
                    if t == 0:
                        pe.wait_ge(w1_in, 32)
                        pe.wait_ge(wd_ready, 1)
                    for n in range(N1):
                        dst = mlp[:, 128 * n:128 * n + 128]
                        nc.tensor.matmul(dst, w1d_sb[:, 0, 128 * n:128 * n + 128],
                                         dnT[:, t, :].rearrange("p (j s) -> p s j", s=4), start=True, stop=False)
                        for c in range(ZC):
                            last = nc.tensor.matmul(dst, w1z_sb[:, c, 128 * n:128 * n + 128], zT[:, c, :],
                                                    start=False, stop=(c == ZC - 1))
                    last.then_inc(top1_done, 1)
                elif kind == "top2":
                    pe.wait_ge(h1_ready, t + 1)
                    if t == 0:
                        pe.wait_ge(w2_in, 16)
                    for m in range(N2):
                        for n in range(N1):
                            last = nc.tensor.matmul(mlp[:, 128 * m:128 * m + 128], w2_sb[:, n, 128 * m:128 * m + 128],
                                                    h1[:, n, :], start=(n == 0), stop=(n == N1 - 1))
                    last.then_inc(top2_done, 1)
                elif kind == "top3":
                    pe.wait_ge(h2_ready, t + 1)
                    if t == 0:
                        pe.wait_ge(small_in, 48)
                    for m in range(N2):
                        last = nc.tensor.matmul(mlp[0:1, 0:128], w3_sb[:, m:m + 1], h2[:, m, :],
                                                start=(m == 0), stop=(m == N2 - 1))
                    last.then_inc(top3_done, 1)


def pair_rows():
    i0, i1 = np.triu_indices(F, k=1)
    row = {(a, b): D + n for n, (a, b) in enumerate(zip(i0.tolist(), i1.tolist()))}
    rows = []
    for g0, n, w in BLOCKS:
        for g in range(g0, g0 + n):
            for f in range(g0 + 1, F):
                pair = (min(SLOTS[g], SLOTS[f]), max(SLOTS[g], SLOTS[f]))
                rows.append(row[pair] if f > g else -1)
    return np.array(rows + [-1] * (128 * ZC - len(rows)))


def kernel(**inputs):
    import concourse.bacc as _bacc
    from concourse import mybir as _mybir
    from concourse.bass_utils import run_bass_kernel_spmd as _run

    a = {n: np.asarray(v) for n, v in inputs.items()}
    ids = a["ids"].reshape(TILES, 4, GRP, NT).transpose(0, 2, 1, 3).reshape(TILES, 128, NT)
    dense = a["r_dense_features"].reshape(TILES, 4, GRP, D).transpose(2, 1, 0, 3).reshape(128, TILES, D)
    one = np.zeros((N_ONEHOT, 128 * R, D), np.float32)
    for i, f in enumerate(ONEHOT):
        one[i, :ROWS[f]] = a[f"tbl_{f}"]
    W1 = a["W_top1"]
    rows = pair_rows()
    w1z = np.zeros((128 * ZC, H1), np.float32)
    w1z[rows >= 0] = W1[rows[rows >= 0]]
    arrays = {f"table_{f}": a[f"tbl_{f}"] for f in GATHERED}
    arrays["onehot_tables"] = one.reshape(N_ONEHOT, 128, R * D)
    arrays["gather_ids"] = ids[:, :, GATHERED].transpose(1, 0, 2).reshape(128, TILES * NG)
    arrays["onehot_ids"] = ids[:, :, ONEHOT].transpose(2, 0, 1).reshape(N_ONEHOT, B)
    arrays["dense"] = dense
    arrays["w1z"] = w1z.reshape(ZC, 128, H1).transpose(1, 0, 2)
    arrays["w1d"] = np.stack([W1[:D], W1[-D:]], axis=1)
    arrays["w2"] = a["W_top2"].reshape(N1, 128, H2).transpose(1, 0, 2)
    arrays["w3"] = a["W_top3"].reshape(N2, 128).T
    arrays["b1"] = a["b_top1"].reshape(N1, 128).T
    arrays["b2"] = a["b_top2"].reshape(N2, 128).T
    arrays = {n: np.ascontiguousarray(v) for n, v in arrays.items()}

    nc = _bacc.Bacc("TRN2", target_bir_lowering=False, num_devices=1)
    ap = {n: nc.dram_tensor(n, v.shape, _mybir.dt.from_np(v.dtype), kind="ExternalInput").ap()
          for n, v in arrays.items()}
    out = nc.dram_tensor("out", (1, B), _mybir.dt.float32, kind="ExternalOutput").ap()
    build(nc, [ap[f"table_{f}"] for f in GATHERED], *(ap[n] for n in (
        "onehot_tables", "gather_ids", "onehot_ids", "dense", "w1z", "w1d", "w2", "w3", "b1", "b2")), out)
    r = _run(nc, [arrays], core_ids=[0])
    return r.results[0]["out"].reshape(B, 1)
```

```python
import numpy as np
import concourse.bass as bass
from concourse import mybir
from contextlib import ExitStack

F32 = mybir.dt.float32
F32R = mybir.dt.float32r
I32 = mybir.dt.int32
ALU = mybir.AluOpType
ACT = mybir.ActivationFunctionType

B, D, NT = 512, 128, 26
ROWS = [1250, 125000, 12500, 1000, 12500, 12500, 1000, 1250, 1000, 1250, 12500, 1250, 12500, 1000,
        12500, 12500, 1000, 12500, 12500, 1000, 1000, 1000, 1000, 1000, 1000, 1000]
N_ONEHOT = 8
SMALL = [f for f in range(NT) if ROWS[f] == 1000]
ONEHOT = SMALL[len(SMALL) - N_ONEHOT:]
GATHERED = [f for f in range(NT) if f not in ONEHOT]
NG = len(GATHERED)
F = NT + 1
SLOTS = [0] + [f + 1 for f in GATHERED + ONEHOT]
TILES = B // 128
CHUNK = 4
CHUNKS = [(c, min(c + CHUNK, NG + 1)) for c in range(0, NG + 1, CHUNK)]
NC_T = len(CHUNKS)
R = 8
GRP = 32
FP = F - 1
PW = 4 * FP
BANKS = GRP // 4
BLOCKS = [(g, n, FP - g) for g, n in [(0, 2), (2, 2)] + [(g, min(4, FP - g)) for g in range(4, FP, 4)]]
ZOFF = [sum(n * w for _, n, w in BLOCKS[:i]) for i in range(len(BLOCKS) + 1)]
ZC = -(-ZOFF[-1] // 128)
H1, H2 = 512, 256
N1, N2 = H1 // 128, H2 // 128


def schedule():
    steps, q = [], 0
    for i in range(N_ONEHOT):
        steps += [("onehot", i), ("chunk", q)]
        q += 1
    for t in range(TILES):
        while q < NC_T * (t + 1):
            steps.append(("chunk", q))
            q += 1
        rest = [[] for _ in range(BANKS)]
        if t:
            half = len(BLOCKS) // 4
            rest = [[("turn", t - 1, k) for k in range(half * i, half * (i + 1))] for i in range(4)]
            rest += [[(s, t - 1)] for s in ("fold", "top1", "top2", "top3")]
        for b in range(BANKS):
            steps.append(("gram", t, b))
            steps += rest[b]
            if t < TILES - 1 and b % 2 == 1 and q < NC_T * (t + 2):
                steps.append(("chunk", q))
                q += 1
    steps += [("turn", TILES - 1, k) for k in range(len(BLOCKS))]
    return steps + [(s, TILES - 1) for s in ("fold", "top1", "top2", "top3")]


STEPS = schedule()
FLIPS = {step: n + 1 for n, step in enumerate(x for x in STEPS if x[0] in ("chunk", "fold"))}
XG_RING = 10
OH_RING = 16
TAB_RING = 3


def build(nc, tables, onehot_tables, gather_ids, onehot_ids, dense, w1z, w1d, w2, w3, b1, b2, out):
    with ExitStack() as ctx:
        def sb(name, shape, dt=F32):
            return ctx.enter_context(nc.sbuf_tensor(name, shape, dt))

        def bank(name):
            return ctx.enter_context(nc.psum_tensor(name, [128, 512], F32))

        def sem(name):
            return ctx.enter_context(nc.semaphore(name))

        xT = sb("xT", [128, TILES, GRP, F, 4])
        tab = sb("tab", [128, TAB_RING, R, D])
        tab_ids = sb("tab_ids", [128, TAB_RING, B], I32)
        th = sb("th", [128, 2, R, D], F32R)
        tl = sb("tl", [128, 2, R, D], F32R)
        oh = sb("oh", [128, OH_RING, B], F32R)
        xg = sb("xg", [128, XG_RING, CHUNK, D])
        dn = sb("dn", [128, TILES, D])
        gids = sb("gids", [128, TILES * NG], I32)
        gram_sb = sb("gram_sb", [PW, 2, 4 * FP, GRP])
        z = sb("z", [128, 128 * ZC])
        zT = sb("zT", [128, ZC, 128])
        w1z_sb = sb("w1z_sb", [128, ZC, H1])
        w1d_sb = sb("w1d_sb", [128, 2, H1])
        w2_sb = sb("w2_sb", [128, N1, H2])
        small = sb("small", [128, N2 + N1 + N2])
        w3_sb, b1_sb, b2_sb = small[:, 0:N2], small[:, N2:N2 + N1], small[:, N2 + N1:]
        h1 = sb("h1", [128, N1, 128])
        h2 = sb("h2", [128, N2, 128])
        ident = sb("ident", [128, 128])
        rowno = sb("rowno", [128, R])
        y = sb("y", [1, B])

        wide = [bank(f"wide{i}") for i in range(4)]
        flip = [bank(f"flip{i}") for i in range(2)]
        prod = [bank(f"prod{i}") for i in range(2)]

        gids_in, dense_in, w1_in, w2_in, small_in = map(sem, ("gids_in", "dense_in", "w1_in", "w2_in", "small_in"))
        tab_in = [sem(f"tab_in{i}") for i in range(TAB_RING)]
        xg_in = [sem(f"xg_in{i}") for i in range(XG_RING)]
        ident_zero, ident_ready, rowno_ready = sem("ident_zero"), sem("ident_ready"), sem("rowno_ready")
        th_ready, tl_ready, oh_ready = sem("th_ready"), sem("tl_ready"), sem("oh_ready")
        oh_used, oh_out = sem("oh_used"), sem("oh_out")
        flipped, flip_out = sem("flipped"), sem("flip_out")
        prod_done, prod_out_act, prod_out_dve = sem("prod_done"), sem("prod_out_act"), sem("prod_out_dve")
        turned, z_act, z_dve = sem("turned"), sem("z_act"), sem("z_dve")
        wd_ready = sem("wd_ready")
        top1_done, h1_act, h1_dve = sem("top1_done"), sem("h1_act"), sem("h1_dve")
        top2_done, h2_act, h2_dve = sem("top2_done"), sem("h2_act"), sem("h2_dve")
        top3_done, y_ready, y_out = sem("top3_done"), sem("y_ready"), sem("y_out")

        def gathers_through(q):
            return sum(CHUNKS[k % NC_T][1] - max(CHUNKS[k % NC_T][0], 1) for k in range(q % XG_RING, q + 1, XG_RING))

        def quadrant_copy(copy, k, s):
            g0, n, w = BLOCKS[k]
            rows = slice(32 * s, 32 * s + 32)
            return copy(z[rows, ZOFF[k]:ZOFF[k + 1]].rearrange("p (g f) -> p g f", f=w),
                        wide[k % 4][rows, 0:128 * n].rearrange("p (g c) -> p g c", c=128)[:, :, 4 * g0 + s:PW:4])

        block = ctx.enter_context(nc.Block())

        @block.sync
        def _(sp):
            def load_table(i):
                if i >= TAB_RING:
                    sp.wait_ge(tl_ready, i - TAB_RING + 1)
                    sp.wait_ge(oh_ready, R * (i - TAB_RING + 1))
                sp.dma_start(tab[:, i % TAB_RING, :, :], onehot_tables[i]).then_inc(tab_in[i % TAB_RING], 16)
                sp.dma_start(tab_ids[:, i % TAB_RING, :],
                             onehot_ids[i:i + 1, :].to_broadcast((128, B))).then_inc(tab_in[i % TAB_RING], 16)

            load_table(0)
            sp.dma_start(gids[:, :], gather_ids).then_inc(gids_in, 16)
            load_table(1)
            sp.dma_start(dn[:, :, :], dense).then_inc(dense_in, 16)
            load_table(2)
            sp.dma_start(w1d_sb[:, :, :], w1d).then_inc(w1_in, 16)
            for i in range(TAB_RING, N_ONEHOT):
                load_table(i)
                if i == TAB_RING:
                    sp.dma_start(w1z_sb[:, :, :], w1z).then_inc(w1_in, 16)
                    sp.dma_start(w2_sb[:, :, :], w2).then_inc(w2_in, 16)
                    sp.dma_start(w3_sb, w3).then_inc(small_in, 16)
                    sp.dma_start(b1_sb, b1).then_inc(small_in, 16)
                    sp.dma_start(b2_sb, b2).then_inc(small_in, 16)
            sp.wait_ge(y_ready, TILES)
            sp.dma_start(out, y[:, :]).then_inc(y_out, 16)
            sp.wait_ge(y_out, 16)

        @block.gpsimd
        def _(pool):
            nc.gpsimd.iota(rowno[:, :], [[1, R]], base=0, channel_multiplier=R,
                           allow_small_or_imprecise_dtypes=True).then_inc(rowno_ready, 1)
            nc.gpsimd.memset(ident[:, :], 0.0).then_inc(ident_zero, 1)
            pool.wait_ge(ident_zero, 1)
            nc.gpsimd.affine_select(out=ident[:, :], in_=ident[:, :], compare_op=ALU.not_equal, fill=1.0, base=0,
                                    pattern=[[-1, 128]], channel_multiplier=1).then_inc(ident_ready, 1)
            pool.wait_ge(gids_in, 16)
            for q in range(TILES * NC_T):
                t, (lo, hi) = q // NC_T, CHUNKS[q % NC_T]
                if q >= XG_RING:
                    pool.wait_ge(flipped, FLIPS["chunk", q - XG_RING])
                for s in range(max(lo, 1), hi):
                    n = t * NG + s - 1
                    pool.indirect_dma_start(xg[:, q % XG_RING, s - lo, :], None, tables[s - 1],
                                            bass.IndirectOffsetOnAxis(ap=gids[:, n:n + 1], axis=0)
                                            ).then_inc(xg_in[q % XG_RING], 16)

        @block.scalar
        def _(act):
            def table_hi(i):
                act.wait_ge(tab_in[i % TAB_RING], 32 * (i // TAB_RING + 1))
                if i >= 2:
                    act.wait_ge(oh_used, R * (i - 1))
                nc.scalar.copy(th[:, i % 2, :, :], tab[:, i % TAB_RING, :, :]).then_inc(th_ready, 1)

            table_hi(0)
            for step in STEPS:
                kind, t = step[0], step[1]
                if kind == "onehot":
                    if t + 1 < N_ONEHOT:
                        table_hi(t + 1)
                    act.wait_ge(oh_used, R * (t + 1))
                    nc.scalar.copy(xT[:, :, :, NG + 1 + t, :].rearrange("p t j s -> p (t j) s"),
                                   wide[t % 4][:, 0:B].rearrange("p (j s) -> p j s", s=4)).then_inc(oh_out, 1)
                elif kind == "chunk":
                    tile, (lo, hi) = t // NC_T, CHUNKS[t % NC_T]
                    act.wait_ge(flipped, FLIPS[step])
                    nc.scalar.copy(xT[:, tile, :, lo:hi, :].rearrange("p j f s -> p f j s"),
                                   flip[FLIPS[step] % 2][:, 0:128 * (hi - lo)].rearrange("p (f j s) -> p f j s", j=GRP, s=4)
                                   ).then_inc(flip_out, 1)
                elif kind == "gram" and step[2] % 2:
                    b = step[2]
                    act.wait_ge(prod_done, BANKS * t + b + 1)
                    if t >= 2:
                        act.wait_ge(turned, len(BLOCKS) * (t - 1))
                    nc.scalar.copy(gram_sb[:, t % 2, :, 4 * b:4 * b + 4],
                                   prod[b % 2][0:PW, 0:4 * PW].rearrange("p (j c) -> p c j", j=4)
                                   ).then_inc(prod_out_act, 1)
                elif kind == "turn":
                    k = step[2]
                    act.wait_ge(turned, len(BLOCKS) * t + k + 1)
                    if t:
                        act.wait_ge(flipped, FLIPS["fold", t - 1])
                    quadrant_copy(nc.scalar.copy, k, 0)
                    quadrant_copy(nc.scalar.copy, k, 1).then_inc(z_act, 1)
                elif kind == "fold":
                    act.wait_ge(flipped, FLIPS[step])
                    nc.scalar.copy(zT[:, :, :],
                                   flip[FLIPS[step] % 2][:, 0:128 * ZC].rearrange("p (c b) -> p c b", b=128)
                                   ).then_inc(flip_out, 1)
                elif kind == "top1":
                    if t == 0:
                        act.wait_ge(small_in, 48)
                    for n in range(0, N1, 2):
                        act.wait_ge(top1_done, N1 * t + n + 1)
                        nc.scalar.activation(h1[:, n, :], wide[n][:, 0:128], ACT.Relu,
                                             bias=b1_sb[:, n:n + 1]).then_inc(h1_act, 1)
                elif kind == "top2":
                    act.wait_ge(top2_done, N2 * t + 1)
                    nc.scalar.activation(h2[:, 0, :], wide[0][:, 0:128], ACT.Relu, bias=b2_sb[:, 0:1]
                                         ).then_inc(h2_act, 1)
                elif kind == "top3":
                    act.wait_ge(top3_done, t + 1)
                    nc.scalar.copy(y[:, 128 * t:128 * t + 128], wide[2][0:1, 0:128]).then_inc(y_ready, 1)

        @block.vector
        def _(dve):
            def build_onehot(i):
                dve.wait_ge(th_ready, i + 1)
                if i >= 2:
                    dve.wait_ge(oh_used, R * (i - 1))
                nc.vector.tensor_tensor(tl[:, i % 2, :, :], tab[:, i % TAB_RING, :, :],
                                        th[:, i % 2, :, :].bitcast(F32), ALU.subtract).then_inc(tl_ready, 1)
                for j in range(R):
                    n = R * i + j
                    if n >= OH_RING:
                        dve.wait_ge(oh_used, n - OH_RING + 1)
                    nc.vector.tensor_scalar(oh[:, n % OH_RING, :], tab_ids[:, i % TAB_RING, :], rowno[:, j:j + 1],
                                            None, ALU.is_equal).then_inc(oh_ready, 1)

            dve.wait_ge(rowno_ready, 1)
            build_onehot(0)
            for step in STEPS:
                kind, t = step[0], step[1]
                if kind == "onehot":
                    if t + 1 < N_ONEHOT:
                        build_onehot(t + 1)
                    else:
                        dve.wait_ge(w1_in, 32)
                        nc.vector.tensor_tensor(w1d_sb[:, 0, :], w1d_sb[:, 0, :], w1d_sb[:, 1, :], ALU.add
                                                ).then_inc(wd_ready, 1)
                elif kind == "gram" and step[2] % 2 == 0:
                    b = step[2]
                    dve.wait_ge(prod_done, BANKS * t + b + 1)
                    if t >= 2:
                        dve.wait_ge(turned, len(BLOCKS) * (t - 1))
                    nc.vector.tensor_copy(gram_sb[:, t % 2, :, 4 * b:4 * b + 4],
                                          prod[b % 2][0:PW, 0:4 * PW].rearrange("p (j c) -> p c j", j=4)
                                          ).then_inc(prod_out_dve, 1)
                elif kind == "turn":
                    k = step[2]
                    dve.wait_ge(turned, len(BLOCKS) * t + k + 1)
                    if t:
                        dve.wait_ge(flipped, FLIPS["fold", t - 1])
                    quadrant_copy(nc.vector.tensor_copy, k, 2)
                    quadrant_copy(nc.vector.tensor_copy, k, 3).then_inc(z_dve, 1)
                elif kind == "top1":
                    if t == 0:
                        dve.wait_ge(small_in, 48)
                    for n in range(1, N1, 2):
                        dve.wait_ge(top1_done, N1 * t + n + 1)
                        nc.vector.tensor_scalar(h1[:, n, :], wide[n][:, 0:128], b1_sb[:, n:n + 1], 0.0,
                                                ALU.add, ALU.max).then_inc(h1_dve, 1)
                elif kind == "top2":
                    dve.wait_ge(top2_done, N2 * t + 2)
                    nc.vector.tensor_scalar(h2[:, 1, :], wide[1][:, 0:128], b2_sb[:, 1:2], 0.0,
                                            ALU.add, ALU.max).then_inc(h2_dve, 1)

        @block.tensor
        def _(pe):
            pe.wait_ge(ident_ready, 1)
            for step in STEPS:
                kind, t = step[0], step[1]
                if kind == "onehot":
                    pe.wait_ge(tl_ready, t + 1)
                    if t >= 4:
                        pe.wait_ge(oh_out, t - 3)
                    acc = wide[t % 4][:, 0:B]
                    for j in range(R):
                        n = R * t + j
                        pe.wait_ge(oh_ready, n + 1)
                        nc.tensor.matmul(acc, th[:, t % 2, j, :], oh[:, n % OH_RING, :], start=(j == 0), stop=False)
                        nc.tensor.matmul(acc, tl[:, t % 2, j, :], oh[:, n % OH_RING, :], start=False,
                                         stop=(j == R - 1)).then_inc(oh_used, 1)
                elif kind == "chunk":
                    tile, (lo, hi) = t // NC_T, CHUNKS[t % NC_T]
                    pe.wait_ge(xg_in[t % XG_RING], 16 * gathers_through(t))
                    if t == 0:
                        pe.wait_ge(dense_in, 16)
                    if FLIPS[step] > 2:
                        pe.wait_ge(flip_out, FLIPS[step] - 2)
                    for s in range(lo, hi):
                        src = dn[:, tile, :] if s == 0 else xg[:, t % XG_RING, s - lo, :]
                        last = nc.tensor.transpose(flip[FLIPS[step] % 2][:, 128 * (s - lo):128 * (s - lo) + 128], src,
                                                   ident[:, :])
                    last.then_inc(flipped, 1)
                elif kind == "gram":
                    b = step[2]
                    if b == 0:
                        pe.wait_ge(flip_out, FLIPS["chunk", NC_T * (t + 1) - 1])
                        pe.wait_ge(oh_out, N_ONEHOT)
                    if BANKS * t + b >= 2:
                        pe.wait_ge(prod_out_act if b % 2 else prod_out_dve, (BANKS * t + b) // 2)
                    for j in range(4 * b, 4 * b + 4):
                        last = nc.tensor.matmul(prod[b % 2][0:PW, PW * (j % 4):PW * (j % 4) + PW],
                                                xT[:, t, j, 1:F, :].rearrange("p f s -> p (f s)"),
                                                xT[:, t, j, 0:FP, :].rearrange("p f s -> p (f s)"),
                                                start=True, stop=True)
                    last.then_inc(prod_done, 1)
                elif kind == "turn":
                    k = step[2]
                    n0 = len(BLOCKS) * t + k
                    if k == 0 and t:
                        pe.wait_ge(y_ready, t)
                    if k == 0:
                        pe.wait_ge(prod_out_act, BANKS // 2 * (t + 1))
                        pe.wait_ge(prod_out_dve, BANKS // 2 * (t + 1))
                    if n0 >= 4:
                        pe.wait_ge(z_act, n0 - 3)
                        pe.wait_ge(z_dve, n0 - 3)
                    g0, n, w = BLOCKS[k]
                    for g in range(n):
                        last = nc.tensor.transpose(
                            wide[k % 4][:, 128 * g:128 * g + PW],
                            gram_sb[:, t % 2, 4 * (g0 + g):4 * (g0 + g) + 4, :].rearrange("p s j -> p (s j)"),
                            ident[0:PW, 0:PW])
                    last.then_inc(turned, 1)
                elif kind == "fold":
                    pe.wait_ge(z_act, len(BLOCKS) * (t + 1))
                    pe.wait_ge(z_dve, len(BLOCKS) * (t + 1))
                    pe.wait_ge(flip_out, FLIPS[step] - 2)
                    for c in range(ZC):
                        last = nc.tensor.transpose(flip[FLIPS[step] % 2][:, 128 * c:128 * c + 128],
                                                   z[:, 128 * c:128 * c + 128], ident[:, :])
                    last.then_inc(flipped, 1)
                elif kind == "top1":
                    if t == 0:
                        pe.wait_ge(w1_in, 32)
                        pe.wait_ge(wd_ready, 1)
                    for n in range(N1):
                        nc.tensor.matmul(wide[n][:, 0:128], w1d_sb[:, 0, 128 * n:128 * n + 128],
                                         xT[:, t, :, 0, :].rearrange("p j s -> p s j"), start=True, stop=False)
                    pe.wait_ge(flip_out, FLIPS["fold", t])
                    for n in range(N1):
                        for c in range(ZC):
                            last = nc.tensor.matmul(wide[n][:, 0:128], w1z_sb[:, c, 128 * n:128 * n + 128],
                                                    zT[:, c, :], start=False, stop=(c == ZC - 1))
                        last.then_inc(top1_done, 1)
                elif kind == "top2":
                    pe.wait_ge(h1_act, N1 // 2 * (t + 1))
                    pe.wait_ge(h1_dve, N1 // 2 * (t + 1))
                    if t == 0:
                        pe.wait_ge(w2_in, 16)
                    for m in range(N2):
                        for n in range(N1):
                            last = nc.tensor.matmul(wide[m][:, 0:128], w2_sb[:, n, 128 * m:128 * m + 128],
                                                    h1[:, n, :], start=(n == 0), stop=(n == N1 - 1))
                        last.then_inc(top2_done, 1)
                elif kind == "top3":
                    if t == 0:
                        pe.wait_ge(small_in, 48)
                    for m in range(N2):
                        pe.wait_ge(h2_dve if m else h2_act, t + 1)
                        last = nc.tensor.matmul(wide[2][0:1, 0:128], w3_sb[:, m:m + 1], h2[:, m, :],
                                                start=(m == 0), stop=(m == N2 - 1))
                    last.then_inc(top3_done, 1)


def pair_rows():
    i0, i1 = np.triu_indices(F, k=1)
    row = {(a, b): D + n for n, (a, b) in enumerate(zip(i0.tolist(), i1.tolist()))}
    rows = []
    for g0, n, w in BLOCKS:
        for g in range(g0, g0 + n):
            for f in range(g0 + 1, F):
                pair = (min(SLOTS[g], SLOTS[f]), max(SLOTS[g], SLOTS[f]))
                rows.append(row[pair] if f > g else -1)
    return np.array(rows + [-1] * (128 * ZC - len(rows)))


def kernel(**inputs):
    import concourse.bacc as _bacc
    from concourse import mybir as _mybir
    from concourse.bass_utils import run_bass_kernel_spmd as _run

    a = {n: np.asarray(v) for n, v in inputs.items()}
    ids = a["ids"].reshape(TILES, 4, GRP, NT).transpose(0, 2, 1, 3).reshape(TILES, 128, NT)
    dense = a["r_dense_features"].reshape(TILES, 4, GRP, D).transpose(2, 1, 0, 3).reshape(128, TILES, D)
    one = np.zeros((N_ONEHOT, 128 * R, D), np.float32)
    for i, f in enumerate(ONEHOT):
        one[i, :ROWS[f]] = a[f"tbl_{f}"]
    W1 = a["W_top1"]
    rows = pair_rows()
    w1z = np.zeros((128 * ZC, H1), np.float32)
    w1z[rows >= 0] = W1[rows[rows >= 0]]
    arrays = {f"table_{f}": a[f"tbl_{f}"] for f in GATHERED}
    arrays["onehot_tables"] = one.reshape(N_ONEHOT, 128, R * D)
    arrays["gather_ids"] = ids[:, :, GATHERED].transpose(1, 0, 2).reshape(128, TILES * NG)
    arrays["onehot_ids"] = ids[:, :, ONEHOT].transpose(2, 0, 1).reshape(N_ONEHOT, B)
    arrays["dense"] = dense
    arrays["w1z"] = w1z.reshape(ZC, 128, H1).transpose(1, 0, 2)
    arrays["w1d"] = np.stack([W1[:D], W1[-D:]], axis=1)
    arrays["w2"] = a["W_top2"].reshape(N1, 128, H2).transpose(1, 0, 2)
    arrays["w3"] = a["W_top3"].reshape(N2, 128).T
    arrays["b1"] = a["b_top1"].reshape(N1, 128).T
    arrays["b2"] = a["b_top2"].reshape(N2, 128).T
    arrays = {n: np.ascontiguousarray(v) for n, v in arrays.items()}

    nc = _bacc.Bacc("TRN2", target_bir_lowering=False, num_devices=1)
    ap = {n: nc.dram_tensor(n, v.shape, _mybir.dt.from_np(v.dtype), kind="ExternalInput").ap()
          for n, v in arrays.items()}
    out = nc.dram_tensor("out", (1, B), _mybir.dt.float32, kind="ExternalOutput").ap()
    build(nc, [ap[f"table_{f}"] for f in GATHERED], *(ap[n] for n in (
        "onehot_tables", "gather_ids", "onehot_ids", "dense", "w1z", "w1d", "w2", "w3", "b1", "b2")), out)
    r = _run(nc, [arrays], core_ids=[0])
    return r.results[0]["out"].reshape(B, 1)
```

```python
import numpy as np
import concourse.bass as bass
from concourse import mybir
from contextlib import ExitStack

F32 = mybir.dt.float32
F32R = mybir.dt.float32r
I32 = mybir.dt.int32
ALU = mybir.AluOpType
ACT = mybir.ActivationFunctionType

B, D, NT = 512, 128, 26
ROWS = [1250, 125000, 12500, 1000, 12500, 12500, 1000, 1250, 1000, 1250, 12500, 1250, 12500, 1000,
        12500, 12500, 1000, 12500, 12500, 1000, 1000, 1000, 1000, 1000, 1000, 1000]
N_ONEHOT = 9
SMALL = [f for f in range(NT) if ROWS[f] == 1000]
ONEHOT = SMALL[len(SMALL) - N_ONEHOT:]
GATHERED = [f for f in range(NT) if f not in ONEHOT]
NG = len(GATHERED)
F = NT + 1
SLOTS = [0] + [f + 1 for f in GATHERED + ONEHOT]
TILES = B // 128
CHUNK = 4
CHUNKS = [(c, min(c + CHUNK, NG + 1)) for c in range(1, NG + 1, CHUNK)]
NC_T = len(CHUNKS)
R = 8
GRP = 32
FP = F - 1
PW = 4 * FP
BANKS = GRP // 4
BLOCKS = [(g, n, g + n - 1) for g, n in [(1, 2)] + [(g, 4) for g in range(3, 23, 4)] + [(23, 2), (25, 2)]]
ZOFF = [sum(n * w for _, n, w in BLOCKS[:i]) for i in range(len(BLOCKS) + 1)]
ZC = -(-ZOFF[-1] // 128)
H1, H2 = 512, 256
N1, N2 = H1 // 128, H2 // 128


COST = {"onehot": 34, "chunk": 5, "gram": 7, "turn": 3, "dense": 9, "fold": 4, "top1": 27, "top2": 18, "top3": 5}
GATHER_COST, FIRST_GATHER, START = 10.4, 50, 57


def schedule():
    steps, now = [], START

    def add(*step):
        nonlocal now
        steps.append(step)
        now += COST[step[0]]

    def next_chunk():
        return sum(s[0] == "chunk" for s in steps)

    def gathered(q):
        tile, c = divmod(q, NC_T)
        return FIRST_GATHER + GATHER_COST * (tile * NG + CHUNKS[c][1] - 1)

    def add_chunk(tile):
        q = next_chunk()
        if q < NC_T * min(tile + 1, TILES) and gathered(q) <= now:
            add("chunk", q)

    for i in range(N_ONEHOT):
        add("onehot", i)
        add_chunk(1)
    for t in range(TILES):
        rest = []
        if t:
            rest = [("turn", t - 1, k) for k in range(len(BLOCKS))]
            rest += [(s, t - 1) for s in ("dense", "fold", "top1", "top2", "top3")]
        while (q := next_chunk()) < NC_T * (t + 1):
            if gathered(q) <= now or not rest:
                now = max(now, gathered(q))
                add("chunk", q)
            else:
                add(*rest.pop(0))
        for b in range(BANKS):
            add("gram", t, b)
            for _ in range(-(-len(rest) // (BANKS - b))):
                add(*rest.pop(0))
            add_chunk(t + 1)
    for k in range(len(BLOCKS)):
        add("turn", TILES - 1, k)
    for s in ("dense", "fold", "top1", "top2", "top3"):
        add(s, TILES - 1)
    return steps


STEPS = schedule()
FLIPS = {step: n + 1 for n, step in enumerate(x for x in STEPS if x[0] in ("chunk", "fold"))}
XG_RING = 10
OH_RING = 16
TAB_RING = 3
WARM_UP = 8


def build(nc, tables, onehot_tables, gather_ids, onehot_ids, dense, w1z, w1d, w2, w3, b1, b2, out):
    with ExitStack() as ctx:
        def sb(name, shape, dt=F32):
            return ctx.enter_context(nc.sbuf_tensor(name, shape, dt))

        def bank(name):
            return ctx.enter_context(nc.psum_tensor(name, [128, 512], F32))

        def sem(name):
            return ctx.enter_context(nc.semaphore(name))

        xT = sb("xT", [128, TILES, GRP, F, 4])
        tab = sb("tab", [128, TAB_RING, R, D])
        tab_ids = sb("tab_ids", [128, TAB_RING, B], I32)
        th = sb("th", [128, 2, R, D], F32R)
        tl = sb("tl", [128, 2, R, D], F32R)
        oh = sb("oh", [128, OH_RING, B], F32R)
        xg = sb("xg", [128, XG_RING, CHUNK, D])
        dnT = sb("dnT", [D, B])
        gids = sb("gids", [128, TILES * NG], I32)
        gram_sb = sb("gram_sb", [PW, 2, 4 * FP, GRP])
        z = sb("z", [128, 128 * ZC])
        zT = sb("zT", [128, ZC, 128])
        w1z_sb = sb("w1z_sb", [128, ZC, H1])
        w1d_sb = sb("w1d_sb", [128, 2, H1])
        w2_sb = sb("w2_sb", [128, N1, H2])
        small = sb("small", [128, N2 + N1 + N2])
        w3_sb, b1_sb, b2_sb = small[:, 0:N2], small[:, N2:N2 + N1], small[:, N2 + N1:]
        h1 = sb("h1", [128, N1, 128])
        h2 = sb("h2", [128, N2, 128])
        ident = sb("ident", [128, 128])
        rowno = sb("rowno", [128, R])
        rowneg = sb("rowneg", [128, 1])
        y = sb("y", [1, B])

        wide = [bank(f"wide{i}") for i in range(4)]
        flip = [bank(f"flip{i}") for i in range(2)]
        prod = [bank(f"prod{i}") for i in range(2)]

        gids_in, dense_in, w1_in, w2_in, small_in = map(sem, ("gids_in", "dense_in", "w1_in", "w2_in", "small_in"))
        first_in, first_ids_in = [sem(f"first_in{i}") for i in range(2)], sem("first_ids_in")
        tab_in = [sem(f"tab_in{i}") for i in range(TAB_RING)]
        xg_in = [sem(f"xg_in{i}") for i in range(XG_RING)]
        ident_zero, ident_ready, rowno_ready = sem("ident_zero"), sem("ident_ready"), sem("rowno_ready")
        rowneg_ready = sem("rowneg_ready")
        th_ready, tl_ready = sem("th_ready"), sem("tl_ready")
        oh_dve, oh_act, distance = sem("oh_dve"), sem("oh_act"), sem("distance")
        oh_used, oh_out = sem("oh_used"), sem("oh_out")
        flipped, flip_out = sem("flipped"), sem("flip_out")
        prod_done, prod_out_act, prod_out_dve = sem("prod_done"), sem("prod_out_act"), sem("prod_out_dve")
        turned, z_act, z_dve = sem("turned"), sem("z_act"), sem("z_dve")
        wd_ready, dense_ready = sem("wd_ready"), sem("dense_ready")
        top1_done, h1_act, h1_dve = sem("top1_done"), sem("h1_act"), sem("h1_dve")
        top2_done, h2_act, h2_dve = sem("top2_done"), sem("h2_act"), sem("h2_dve")
        top3_done, y_ready, y_out = sem("top3_done"), sem("y_ready"), sem("y_out")

        def tab_count(i):
            return 32 * (i // TAB_RING + (i % TAB_RING > 0))

        def gathers_through(q):
            return sum(CHUNKS[k % NC_T][1] - CHUNKS[k % NC_T][0] for k in range(q % XG_RING, q + 1, XG_RING))

        def quadrant_copy(copy, k, s):
            g0, n, w = BLOCKS[k]
            rows = slice(32 * s, 32 * s + 32)
            return copy(z[rows, ZOFF[k]:ZOFF[k + 1]].rearrange("p (g f) -> p g f", f=w),
                        wide[k % 4][rows, 0:128 * n].rearrange("p (g c) -> p g c", c=128)[:, :, s:4 * w:4])

        block = ctx.enter_context(nc.Block())

        @block.sync
        def _(sp):
            def load_table(i):
                if i >= TAB_RING:
                    sp.wait_ge(tl_ready, i - TAB_RING + 4)
                    sp.wait_ge(oh_dve, (R - 1) * (i - TAB_RING + 1))
                    sp.wait_ge(oh_act, i - TAB_RING + 1)
                sp.dma_start(tab_ids[:, i % TAB_RING, :],
                             onehot_ids[i:i + 1, :].to_broadcast((128, B))).then_inc(tab_in[i % TAB_RING], 16)
                sp.dma_start(tab[:, i % TAB_RING, :, :], onehot_tables[i]).then_inc(tab_in[i % TAB_RING], 16)

            sp.dma_start(gids[:, :], gather_ids).then_inc(gids_in, 16)
            for half in range(2):
                rows = slice(R // 2 * half, R // 2 * (half + 1))
                sp.dma_start(tab[:, 0, rows, :], onehot_tables[0][:, rows, :]).then_inc(first_in[half], 16)
            load_table(1)
            sp.dma_start(dnT[:, :], dense).then_inc(dense_in, 16)
            load_table(2)
            for i in range(TAB_RING, N_ONEHOT):
                load_table(i)
            sp.dma_start(w1d_sb[:, :, :], w1d).then_inc(w1_in, 16)
            sp.dma_start(w1z_sb[:, :, :], w1z).then_inc(w1_in, 16)
            sp.dma_start(w2_sb[:, :, :], w2).then_inc(w2_in, 16)
            sp.dma_start(w3_sb, w3).then_inc(small_in, 16)
            sp.dma_start(b1_sb, b1).then_inc(small_in, 16)
            sp.dma_start(b2_sb, b2).then_inc(small_in, 16)
            sp.wait_ge(y_ready, TILES)
            sp.dma_start(out, y[:, :]).then_inc(y_out, 16)
            sp.wait_ge(y_out, 16)

        @block.gpsimd
        def _(pool):
            nc.gpsimd.iota(rowno[:, :], [[1, R]], base=0, channel_multiplier=R,
                           allow_small_or_imprecise_dtypes=True).then_inc(rowno_ready, 1)
            nc.gpsimd.memset(ident[:, :], 0.0).then_inc(ident_zero, 1)
            pool.wait_ge(ident_zero, 1)
            nc.gpsimd.affine_select(out=ident[:, :], in_=ident[:, :], compare_op=ALU.not_equal, fill=1.0, base=0,
                                    pattern=[[-1, 128]], channel_multiplier=1).then_inc(ident_ready, 1)
            pool.wait_ge(gids_in, 16)
            for q in range(TILES * NC_T):
                t, (lo, hi) = q // NC_T, CHUNKS[q % NC_T]
                if q >= XG_RING:
                    pool.wait_ge(flipped, FLIPS["chunk", q - XG_RING])
                for s in range(lo, hi):
                    n = t * NG + s - 1
                    pool.indirect_dma_start(xg[:, q % XG_RING, s - lo, :], None, tables[s - 1],
                                            bass.IndirectOffsetOnAxis(ap=gids[:, n:n + 1], axis=0)
                                            ).then_inc(xg_in[q % XG_RING], 16)

        @block.scalar
        def _(act):
            def table_hi(i):
                if i:
                    act.wait_ge(tab_in[i % TAB_RING], tab_count(i))
                if i >= 2:
                    act.wait_ge(oh_used, R * (i - 1))
                for r in range(0, R, R if i else R // 4):
                    part = slice(r, r + (R if i else R // 4))
                    if i == 0:
                        act.wait_ge(first_in[r // (R // 2)], 16)
                    nc.scalar.copy(th[:, i % 2, part, :], tab[:, i % TAB_RING, part, :]).then_inc(th_ready, 1)

            def last_onehot(i):
                n = R * i + R - 1
                if n >= OH_RING:
                    act.wait_ge(oh_used, n - OH_RING + 1)
                nc.scalar.activation(oh[:, n % OH_RING, :], tab_ids[:, i % TAB_RING, :], ACT.Abs,
                                     bias=rowneg[:, :]).then_inc(distance, 1)
                act.wait_ge(distance, i + 1)
                nc.scalar.activation(oh[:, n % OH_RING, :], oh[:, n % OH_RING, :].bitcast(F32), ACT.Relu,
                                     bias=1.0, scale=-1.0).then_inc(oh_act, 1)

            act.dma_start(tab_ids[:, 0, :], onehot_ids[0:1, :].to_broadcast((128, B))).then_inc(first_ids_in, 16)
            act.wait_ge(rowno_ready, 1)
            nc.scalar.mul(rowneg[:, :], rowno[:, R - 1:R], -1.0).then_inc(rowneg_ready, 1)
            table_hi(0)
            act.wait_ge(rowneg_ready, 1)
            act.wait_ge(first_ids_in, 16)
            last_onehot(0)
            for step in STEPS:
                kind, t = step[0], step[1]
                if kind == "onehot":
                    if t + 1 < N_ONEHOT:
                        table_hi(t + 1)
                        last_onehot(t + 1)
                    act.wait_ge(oh_used, R * (t + 1))
                    nc.scalar.copy(xT[:, :, :, NG + 1 + t, :].rearrange("p t j s -> p (t j) s"),
                                   wide[t % 4][:, 0:B].rearrange("p (j s) -> p j s", s=4)).then_inc(oh_out, 1)
                elif kind == "chunk":
                    tile, (lo, hi) = t // NC_T, CHUNKS[t % NC_T]
                    act.wait_ge(flipped, FLIPS[step])
                    nc.scalar.copy(xT[:, tile, :, lo:hi, :].rearrange("p j f s -> p f j s"),
                                   flip[FLIPS[step] % 2][:, 0:128 * (hi - lo)].rearrange("p (f j s) -> p f j s", j=GRP, s=4)
                                   ).then_inc(flip_out, 1)
                elif kind == "gram" and step[2] % 2:
                    b = step[2]
                    act.wait_ge(prod_done, BANKS * t + b + 1)
                    if t >= 2:
                        act.wait_ge(turned, len(BLOCKS) * (t - 1))
                    nc.scalar.copy(gram_sb[:, t % 2, :, 4 * b:4 * b + 4],
                                   prod[b % 2][0:PW, 0:4 * PW].rearrange("p (j c) -> p c j", j=4)
                                   ).then_inc(prod_out_act, 1)
                elif kind == "turn":
                    k = step[2]
                    act.wait_ge(turned, len(BLOCKS) * t + k + 1)
                    if t:
                        act.wait_ge(flipped, FLIPS["fold", t - 1])
                    quadrant_copy(nc.scalar.copy, k, 0)
                    quadrant_copy(nc.scalar.copy, k, 1).then_inc(z_act, 1)
                elif kind == "fold":
                    act.wait_ge(flipped, FLIPS[step])
                    nc.scalar.copy(zT[:, :, :],
                                   flip[FLIPS[step] % 2][:, 0:128 * ZC].rearrange("p (c b) -> p c b", b=128)
                                   ).then_inc(flip_out, 1)
                elif kind == "top1":
                    if t == 0:
                        act.wait_ge(small_in, 48)
                    for n in range(0, N1, 2):
                        act.wait_ge(top1_done, N1 * t + n + 1)
                        nc.scalar.activation(h1[:, n, :], wide[n][:, 0:128], ACT.Relu,
                                             bias=b1_sb[:, n:n + 1]).then_inc(h1_act, 1)
                elif kind == "top2":
                    act.wait_ge(top2_done, N2 * t + 1)
                    nc.scalar.activation(h2[:, 0, :], wide[0][:, 0:128], ACT.Relu, bias=b2_sb[:, 0:1]
                                         ).then_inc(h2_act, 1)
                elif kind == "top3":
                    act.wait_ge(top3_done, t + 1)
                    nc.scalar.copy(y[:, 128 * t:128 * t + 128], wide[2][0:1, 0:128]).then_inc(y_ready, 1)

        @block.vector
        def _(dve):
            def table_lo(i, part):
                nc.vector.tensor_tensor(tl[:, i % 2, part, :], tab[:, i % TAB_RING, part, :],
                                        th[:, i % 2, part, :].bitcast(F32), ALU.subtract).then_inc(tl_ready, 1)

            def onehot_columns(i, j):
                n = R * i + j
                if n >= OH_RING:
                    dve.wait_ge(oh_used, n - OH_RING + 1)
                nc.vector.tensor_scalar(oh[:, n % OH_RING, :], tab_ids[:, i % TAB_RING, :], rowno[:, j:j + 1],
                                        None, ALU.is_equal).then_inc(oh_dve, 1)

            def build_onehot(i):
                dve.wait_ge(th_ready, i + 4)
                if i >= 2:
                    dve.wait_ge(oh_used, R * (i - 1))
                table_lo(i, slice(0, R))
                for j in range(R - 1):
                    onehot_columns(i, j)

            dve.wait_ge(rowno_ready, 1)
            dve.wait_ge(first_ids_in, 16)
            for part in range(4):
                for j in range(R // 4 * part, min(R // 4 * (part + 1), R - 1)):
                    onehot_columns(0, j)
                dve.wait_ge(th_ready, part + 1)
                table_lo(0, slice(R // 4 * part, R // 4 * (part + 1)))
            for step in STEPS:
                kind, t = step[0], step[1]
                if kind == "onehot":
                    if t + 1 < N_ONEHOT:
                        build_onehot(t + 1)
                    else:
                        dve.wait_ge(dense_in, 16)
                        nc.vector.tensor_copy(xT[:, :, :, 0, :].rearrange("p t j s -> p (t j) s"),
                                              dnT[:, :].rearrange("p (j s) -> p j s", s=4)).then_inc(dense_ready, 1)
                        dve.wait_ge(w1_in, 32)
                        nc.vector.tensor_tensor(w1d_sb[:, 0, :], w1d_sb[:, 0, :], w1d_sb[:, 1, :], ALU.add
                                                ).then_inc(wd_ready, 1)
                elif kind == "gram" and step[2] % 2 == 0:
                    b = step[2]
                    dve.wait_ge(prod_done, BANKS * t + b + 1)
                    if t >= 2:
                        dve.wait_ge(turned, len(BLOCKS) * (t - 1))
                    nc.vector.tensor_copy(gram_sb[:, t % 2, :, 4 * b:4 * b + 4],
                                          prod[b % 2][0:PW, 0:4 * PW].rearrange("p (j c) -> p c j", j=4)
                                          ).then_inc(prod_out_dve, 1)
                elif kind == "turn":
                    k = step[2]
                    dve.wait_ge(turned, len(BLOCKS) * t + k + 1)
                    if t:
                        dve.wait_ge(flipped, FLIPS["fold", t - 1])
                    quadrant_copy(nc.vector.tensor_copy, k, 2)
                    quadrant_copy(nc.vector.tensor_copy, k, 3).then_inc(z_dve, 1)
                elif kind == "top1":
                    if t == 0:
                        dve.wait_ge(small_in, 48)
                    for n in range(1, N1, 2):
                        dve.wait_ge(top1_done, N1 * t + n + 1)
                        nc.vector.tensor_scalar(h1[:, n, :], wide[n][:, 0:128], b1_sb[:, n:n + 1], 0.0,
                                                ALU.add, ALU.max).then_inc(h1_dve, 1)
                elif kind == "top2":
                    dve.wait_ge(top2_done, N2 * t + 2)
                    nc.vector.tensor_scalar(h2[:, 1, :], wide[1][:, 0:128], b2_sb[:, 1:2], 0.0,
                                            ALU.add, ALU.max).then_inc(h2_dve, 1)

        @block.tensor
        def _(pe):
            pe.wait_ge(ident_ready, 1)
            for _ in range(WARM_UP):
                nc.tensor.matmul(prod[0][:, 0:128], ident[:, :], ident[:, :], start=True, stop=True)
            for step in STEPS:
                kind, t = step[0], step[1]
                if kind == "onehot":
                    if t:
                        pe.wait_ge(tl_ready, t + 4)
                    if t >= 4:
                        pe.wait_ge(oh_out, t - 3)
                    acc = wide[t % 4][:, 0:B]
                    for j in range(R):
                        n = R * t + j
                        if t == 0:
                            pe.wait_ge(tl_ready, j // (R // 4) + 1)
                        if j < R - 1:
                            pe.wait_ge(oh_dve, (R - 1) * t + j + 1)
                        else:
                            pe.wait_ge(oh_act, t + 1)
                        nc.tensor.matmul(acc, th[:, t % 2, j, :], oh[:, n % OH_RING, :], start=(j == 0), stop=False)
                        nc.tensor.matmul(acc, tl[:, t % 2, j, :], oh[:, n % OH_RING, :], start=False,
                                         stop=(j == R - 1)).then_inc(oh_used, 1)
                elif kind == "chunk":
                    tile, (lo, hi) = t // NC_T, CHUNKS[t % NC_T]
                    pe.wait_ge(xg_in[t % XG_RING], 16 * gathers_through(t))
                    if FLIPS[step] > 2:
                        pe.wait_ge(flip_out, FLIPS[step] - 2)
                    for s in range(lo, hi):
                        last = nc.tensor.transpose(flip[FLIPS[step] % 2][:, 128 * (s - lo):128 * (s - lo) + 128],
                                                   xg[:, t % XG_RING, s - lo, :], ident[:, :])
                    last.then_inc(flipped, 1)
                elif kind == "gram":
                    b = step[2]
                    if b == 0:
                        pe.wait_ge(flip_out, FLIPS["chunk", NC_T * (t + 1) - 1])
                        pe.wait_ge(oh_out, N_ONEHOT)
                        pe.wait_ge(dense_ready, 1)
                    if BANKS * t + b >= 2:
                        pe.wait_ge(prod_out_act if b % 2 else prod_out_dve, (BANKS * t + b) // 2)
                    for j in range(4 * b, 4 * b + 4):
                        last = nc.tensor.matmul(prod[b % 2][0:PW, PW * (j % 4):PW * (j % 4) + PW],
                                                xT[:, t, j, 0:FP, :].rearrange("p f s -> p (f s)"),
                                                xT[:, t, j, 1:F, :].rearrange("p f s -> p (f s)"),
                                                start=True, stop=True)
                    last.then_inc(prod_done, 1)
                elif kind == "turn":
                    k = step[2]
                    n0 = len(BLOCKS) * t + k
                    if k == 0 and t:
                        pe.wait_ge(y_ready, t)
                    if k == 0:
                        pe.wait_ge(prod_out_act, BANKS // 2 * (t + 1))
                        pe.wait_ge(prod_out_dve, BANKS // 2 * (t + 1))
                    if n0 >= 4:
                        pe.wait_ge(z_act, n0 - 3)
                        pe.wait_ge(z_dve, n0 - 3)
                    g0, n, w = BLOCKS[k]
                    rows = max(4 * w, 68)
                    for g in range(n):
                        col = 4 * (g0 + g - 1)
                        last = nc.tensor.transpose(
                            wide[k % 4][:, 128 * g:128 * g + rows],
                            gram_sb[0:rows, t % 2, col:col + 4, :].rearrange("p s j -> p (s j)"),
                            ident[0:rows, 0:rows])
                    last.then_inc(turned, 1)
                elif kind == "fold":
                    pe.wait_ge(z_act, len(BLOCKS) * (t + 1))
                    pe.wait_ge(z_dve, len(BLOCKS) * (t + 1))
                    pe.wait_ge(flip_out, FLIPS[step] - 2)
                    for c in range(ZC):
                        last = nc.tensor.transpose(flip[FLIPS[step] % 2][:, 128 * c:128 * c + 128],
                                                   z[:, 128 * c:128 * c + 128], ident[:, :])
                    last.then_inc(flipped, 1)
                elif kind == "dense":
                    if t == 0:
                        pe.wait_ge(w1_in, 32)
                        pe.wait_ge(wd_ready, 1)
                    for n in range(N1):
                        last_block = len(BLOCKS) * t + len(BLOCKS) - 4 + n
                        pe.wait_ge(z_act, last_block + 1)
                        pe.wait_ge(z_dve, last_block + 1)
                        nc.tensor.matmul(wide[n][:, 0:128], w1d_sb[:, 0, 128 * n:128 * n + 128],
                                         dnT[:, 128 * t:128 * t + 128].rearrange("p (j s) -> p s j", s=4),
                                         start=True, stop=False)
                elif kind == "top1":
                    pe.wait_ge(flip_out, FLIPS["fold", t])
                    for n in range(N1):
                        for c in range(ZC):
                            last = nc.tensor.matmul(wide[n][:, 0:128], w1z_sb[:, c, 128 * n:128 * n + 128],
                                                    zT[:, c, :], start=False, stop=(c == ZC - 1))
                        last.then_inc(top1_done, 1)
                elif kind == "top2":
                    if t == 0:
                        pe.wait_ge(w2_in, 16)
                    for n, m in [(n, m) for m in range(N2) for n in range(N1 - 1)] + [(N1 - 1, m) for m in range(N2)]:
                        pe.wait_ge(h1_dve if n % 2 else h1_act, N1 // 2 * t + n // 2 + 1)
                        if m:
                            pe.wait_ge(h1_dve, N1 // 2 * t + 1)
                        last = nc.tensor.matmul(wide[m][:, 0:128], w2_sb[:, n, 128 * m:128 * m + 128],
                                                h1[:, n, :], start=(n == 0), stop=(n == N1 - 1))
                        if n == N1 - 1:
                            last.then_inc(top2_done, 1)
                elif kind == "top3":
                    if t == 0:
                        pe.wait_ge(small_in, 48)
                    for m in range(N2):
                        pe.wait_ge(h2_dve if m else h2_act, t + 1)
                        last = nc.tensor.matmul(wide[2][0:1, 0:128], w3_sb[:, m:m + 1], h2[:, m, :],
                                                start=(m == 0), stop=(m == N2 - 1))
                    last.then_inc(top3_done, 1)


def pair_rows():
    i0, i1 = np.triu_indices(F, k=1)
    row = {(a, b): D + n for n, (a, b) in enumerate(zip(i0.tolist(), i1.tolist()))}
    rows = []
    for g0, n, w in BLOCKS:
        for g in range(g0, g0 + n):
            for f in range(w):
                pair = (min(SLOTS[g], SLOTS[f]), max(SLOTS[g], SLOTS[f]))
                rows.append(row[pair] if f < g else -1)
    return np.array(rows + [-1] * (128 * ZC - len(rows)))


def kernel(**inputs):
    import concourse.bacc as _bacc
    from concourse import mybir as _mybir
    from concourse.bass_utils import run_bass_kernel_spmd as _run

    a = {n: np.asarray(v) for n, v in inputs.items()}
    ids = a["ids"].reshape(TILES, 4, GRP, NT).transpose(0, 2, 1, 3).reshape(TILES, 128, NT)
    dense = a["r_dense_features"].reshape(TILES, 4, GRP, D).transpose(3, 0, 2, 1).reshape(D, B)
    one = np.zeros((N_ONEHOT, 128 * R, D), np.float32)
    for i, f in enumerate(ONEHOT):
        one[i, :ROWS[f]] = a[f"tbl_{f}"]
    W1 = a["W_top1"]
    rows = pair_rows()
    w1z = np.zeros((128 * ZC, H1), np.float32)
    w1z[rows >= 0] = W1[rows[rows >= 0]]
    arrays = {f"table_{f}": a[f"tbl_{f}"] for f in GATHERED}
    arrays["onehot_tables"] = one.reshape(N_ONEHOT, 128, R, D)
    arrays["gather_ids"] = ids[:, :, GATHERED].transpose(1, 0, 2).reshape(128, TILES * NG)
    arrays["onehot_ids"] = ids[:, :, ONEHOT].transpose(2, 0, 1).reshape(N_ONEHOT, B)
    arrays["dense"] = dense
    arrays["w1z"] = w1z.reshape(ZC, 128, H1).transpose(1, 0, 2)
    arrays["w1d"] = np.stack([W1[:D], W1[-D:]], axis=1)
    arrays["w2"] = a["W_top2"].reshape(N1, 128, H2).transpose(1, 0, 2)
    arrays["w3"] = a["W_top3"].reshape(N2, 128).T
    arrays["b1"] = a["b_top1"].reshape(N1, 128).T
    arrays["b2"] = a["b_top2"].reshape(N2, 128).T
    arrays = {n: np.ascontiguousarray(v) for n, v in arrays.items()}

    nc = _bacc.Bacc("TRN2", target_bir_lowering=False, num_devices=1)
    ap = {n: nc.dram_tensor(n, v.shape, _mybir.dt.from_np(v.dtype), kind="ExternalInput").ap()
          for n, v in arrays.items()}
    out = nc.dram_tensor("out", (1, B), _mybir.dt.float32, kind="ExternalOutput").ap()
    build(nc, [ap[f"table_{f}"] for f in GATHERED], *(ap[n] for n in (
        "onehot_tables", "gather_ids", "onehot_ids", "dense", "w1z", "w1d", "w2", "w3", "b1", "b2")), out)
    r = _run(nc, [arrays], core_ids=[0])
    return r.results[0]["out"].reshape(B, 1)
```
